# Optimizing a Trainium2 kernel written in Bass

```python
import numpy as np
import jax
import jax.numpy as jnp

def _softmax(x, axis=-1):
    return jax.nn.softmax(x, axis=axis)

def _gelu(x):
    return jax.nn.gelu(x, approximate=True)

def _silu(x):
    return jax.nn.silu(x)

def _sigmoid(x):
    return jax.nn.sigmoid(x)

def _layernorm(x, axis=-1, eps=1e-05):
    m = jnp.mean(x, axis=axis, keepdims=True)
    v = jnp.var(x, axis=axis, keepdims=True)
    return (x - m) / jnp.sqrt(v + eps)

def _scatter_add(tgt, idx, src, axis=0):
    return tgt.at[idx].add(src)

def _segment_sum(src, seg, n):
    return jax.ops.segment_sum(src, seg, n)
kernel_name = 'mk_cond_resid_d2_seqx_r4_1973ed'

def setup_inputs(seed: int=0):
    np.random.seed(seed)
    _w = jnp.asarray

    def _rec_inputs():
        import jax
        import jax.numpy as jnp
        _rk = jax.random.key(seed)
        x = -0.000125 + 0.9999 * jax.random.normal(jax.random.fold_in(_rk, 1), (2, 1024, 256), jnp.float32)
        _lenS = 1024 - jax.random.randint(jax.random.fold_in(_rk, 7), (2,), 0, max(1, 1024 // 4) + 1, jnp.int32)
        _lenS2 = 1024 - jax.random.randint(jax.random.fold_in(_rk, 8), (2,), 0, max(1, 1024 // 4) + 1, jnp.int32)
        cond_1024 = -0.00493535 + 1.00056 * jax.random.normal(jax.random.fold_in(_rk, 11), (2, 256), jnp.float32)
        return (x, cond_1024)
    x, cond_1024 = _rec_inputs()

    def _L0_cond_setup():
        import jax, jax.numpy as jnp
        import numpy as np
        N, T, D, H = (64, 128, 256, 256)

        def lstm_scan(x, h0, Wx, Wh, b):
            xW = jnp.einsum('ntd,dg->ntg', x, Wx) + b
            Hdim = h0.shape[1]
            c0 = jnp.zeros_like(h0)

            def step(carry, xw_t):
                prev_h, prev_c = carry
                a = xw_t + prev_h @ Wh
                i = jax.nn.sigmoid(a[:, :Hdim])
                f = jax.nn.sigmoid(a[:, Hdim:2 * Hdim])
                o = jax.nn.sigmoid(a[:, 2 * Hdim:3 * Hdim])
                g = jnp.tanh(a[:, 3 * Hdim:])
                next_c = f * prev_c + i * g
                next_h = o * jnp.tanh(next_c)
                return ((next_h, next_c), next_h)
            _, hs = jax.lax.scan(step, (h0, c0), jnp.swapaxes(xW, 0, 1))
            return jnp.swapaxes(hs, 0, 1)
        key = jax.random.key(seed)
        k1, k2, k3, k4 = jax.random.split(key, 4)
        x = jax.random.normal(k1, (N, T, D), dtype=jnp.float32)
        h0 = jax.random.normal(k2, (N, H), dtype=jnp.float32)
        Wx = jax.random.normal(k3, (D, 4 * H), dtype=jnp.float32) / np.sqrt(D)
        Wh = jax.random.normal(k4, (H, 4 * H), dtype=jnp.float32) / np.sqrt(H)
        b = jnp.zeros((4 * H,), dtype=jnp.float32)
        return {'x': x, 'h0': h0, 'Wx': Wx, 'Wh': Wh, 'b': b}
    _L0_cond_all = _L0_cond_setup()
    _L0_cond_in = {k: v for k, v in _L0_cond_all.items() if k in ('Wx', 'Wh', 'b')}
    del _L0_cond_all

    def _L1_cond_setup():
        import jax, jax.numpy as jnp
        import numpy as np
        from jax import lax
        ALPHA_LO = float(np.exp(-1.0 / 5.0))
        ALPHA_HI = float(np.exp(-1.0 / 25.0))
        THRESHOLD = 1.0

        @jax.custom_vjp
        def spike_boxcar(x):
            return (x > 0).astype(x.dtype)

        def _spike_fwd(x):
            return (spike_boxcar(x), x)

        def _spike_bwd(x, g):
            mask = ((x > -0.5) & (x <= 0.5)).astype(g.dtype)
            return (g * mask,)
        spike_boxcar.defvjp(_spike_fwd, _spike_bwd)
        key = jax.random.key(seed)
        kx, kW, kV, ka, ku, ks = jax.random.split(key, 6)
        B, T, I, H = (64, 250, 256, 256)
        x = jax.random.normal(kx, (B, T, I), dtype=jnp.float32)
        W = jax.random.normal(kW, (H, I), dtype=jnp.float32) / np.sqrt(I)
        V = jnp.linalg.qr(jax.random.normal(kV, (H, H), dtype=jnp.float32))[0]
        alpha = jax.random.uniform(ka, (H,), dtype=jnp.float32, minval=ALPHA_LO, maxval=ALPHA_HI)
        ut0 = jax.random.uniform(ku, (B, H), dtype=jnp.float32)
        st0 = jax.random.uniform(ks, (B, H), dtype=jnp.float32)
        return {'x': x, 'W': W, 'V': V, 'alpha': alpha, 'ut0': ut0, 'st0': st0}
    _L1_cond_all = _L1_cond_setup()
    _L1_cond_in = {k: v for k, v in _L1_cond_all.items() if k in ('W', 'V', 'alpha')}
    del _L1_cond_all
    return {'x': x, 'cond_1024': cond_1024, 'L0_cond_Wx': _L0_cond_in['Wx'], 'L0_cond_Wh': _L0_cond_in['Wh'], 'L0_cond_b': _L0_cond_in['b'], 'L1_cond_W': _L1_cond_in['W'], 'L1_cond_V': _L1_cond_in['V'], 'L1_cond_alpha': _L1_cond_in['alpha']}

def reference(x, cond_1024, L0_cond_Wx, L0_cond_Wh, L0_cond_b, L1_cond_W, L1_cond_V, L1_cond_alpha):
    import jax
    import jax.numpy as jnp

    def _L0_cond_ref(x, h0, Wx, Wh, b):
        import jax, jax.numpy as jnp
        import numpy as np
        N, T, D, H = (64, 128, 256, 256)

        def lstm_scan(x, h0, Wx, Wh, b):
            xW = jnp.einsum('ntd,dg->ntg', x, Wx) + b
            Hdim = h0.shape[1]
            c0 = jnp.zeros_like(h0)

            def step(carry, xw_t):
                prev_h, prev_c = carry
                a = xw_t + prev_h @ Wh
                i = jax.nn.sigmoid(a[:, :Hdim])
                f = jax.nn.sigmoid(a[:, Hdim:2 * Hdim])
                o = jax.nn.sigmoid(a[:, 2 * Hdim:3 * Hdim])
                g = jnp.tanh(a[:, 3 * Hdim:])
                next_c = f * prev_c + i * g
                next_h = o * jnp.tanh(next_c)
                return ((next_h, next_c), next_h)
            _, hs = jax.lax.scan(step, (h0, c0), jnp.swapaxes(xW, 0, 1))
            return jnp.swapaxes(hs, 0, 1)
        return lstm_scan(x, h0, Wx, Wh, b)

    def _L1_cond_ref(x, W, V, alpha, ut0, st0):
        import jax, jax.numpy as jnp
        import numpy as np
        from jax import lax
        ALPHA_LO = float(np.exp(-1.0 / 5.0))
        ALPHA_HI = float(np.exp(-1.0 / 25.0))
        THRESHOLD = 1.0

        @jax.custom_vjp
        def spike_boxcar(x):
            return (x > 0).astype(x.dtype)

        def _spike_fwd(x):
            return (spike_boxcar(x), x)

        def _spike_bwd(x, g):
            mask = ((x > -0.5) & (x <= 0.5)).astype(g.dtype)
            return (g * mask,)
        spike_boxcar.defvjp(_spike_fwd, _spike_bwd)
        Wx = jnp.einsum('bti,hi->bth', x, W)
        a = jnp.clip(alpha, ALPHA_LO, ALPHA_HI)
        H = V.shape[0]
        Vz = V * (1.0 - jnp.eye(H, dtype=V.dtype))

        def step(carry, wx_t):
            ut, st = carry
            ut = a * (ut - st) + (1.0 - a) * (wx_t + st @ Vz)
            st = spike_boxcar(ut - THRESHOLD)
            return ((ut, st), st)
        Wx_t = jnp.swapaxes(Wx, 0, 1)
        _, s = lax.scan(step, (ut0, st0), Wx_t)
        return jnp.swapaxes(s, 0, 1)
    x = x + _L0_cond_ref(x, cond_1024, L0_cond_Wx, L0_cond_Wh, L0_cond_b)
    x = x + _L1_cond_ref(x, L1_cond_W, L1_cond_V, L1_cond_alpha, cond_1024, cond_1024)
    return x

_drawn_inputs = setup_inputs


def setup_inputs(seed=0):
    import zlib

    import numpy as np

    out = dict(_drawn_inputs(seed))
    spreads = {'L0_cond_b': (0.0, 0.1)}
    factors = {'cond_1024': 8.0, 'L1_cond_W': 2.776, 'L1_cond_V': 8.0, 'L1_cond_alpha': 3.639}
    for name, (base, spread) in spreads.items():
        noise = np.random.default_rng([zlib.crc32(name.encode()), seed]).standard_normal(out[name].shape)
        drawn = base * np.exp(spread * noise) if base else spread * noise
        out[name] = jnp.asarray(drawn.astype(out[name].dtype))
    for name, factor in factors.items():
        out[name] = (out[name] * factor).astype(out[name].dtype)
    return out
```

```python
from contextlib import ExitStack

import numpy as np

import concourse.bass as bass
import concourse.mybir as mybir

F32 = mybir.dt.float32
ALU = mybir.AluOpType
ACT = mybir.ActivationFunctionType

BATCH, TIME, HID = 2, 1024, 256
C = 32
GROUPS = 4
HB = HID // GROUPS
HALVES = HB // C
GATES = 4
ZW = GATES * HB
STEPS = C // BATCH
CHUNKS = TIME // STEPS
assert STEPS == 16
KB = HALVES * BATCH
ALPHA_LO = float(np.exp(-1.0 / 5.0))
ALPHA_HI = float(np.exp(-1.0 / 25.0))
THRESHOLD = 1.0
XRAW_SLOT, XT_SLOT = 8, 12


def build(nc, x, cond, wx, wh, bias, wt, v, eye, noteye, ident, alpha_row, alpha_unit, out):
    with ExitStack() as ctx:
        def sb(name, shape):
            return ctx.enter_context(nc.sbuf_tensor(name, shape, F32))

        def bank(name):
            return ctx.enter_context(nc.psum_tensor(name, [128, 512], F32))

        def sem(name):
            return ctx.enter_context(nc.semaphore(name))

        wx_sb = sb("wx_sb", [128, HALVES, GROUPS, ZW])
        wh_sb = sb("wh_sb", [128, HALVES, GROUPS, ZW])
        bias_sb = sb("bias_sb", [128, ZW])
        wt_sb = sb("wt_sb", [128, HALVES, HID])
        v_sb = sb("v_sb", [128, HALVES, HID])
        eye_sb = sb("eye_sb", [128, HALVES, HID])
        noteye_sb = sb("noteye_sb", [128, HALVES, HID])
        ident_sb = sb("ident_sb", [128, 128])
        a_row = sb("a_row", [128, HID])
        oma_row = sb("oma_row", [128, HID])
        a_raw = sb("a_raw", [128, HALVES])
        a_unit = sb("a_unit", [128, KB])
        cond_sb = sb("cond_sb", [128, KB])
        x_row = sb("x_row", [128, HB])
        xt_next = sb("xt_next", [128, HALVES * C])
        xt_now = sb("xt_now", [128, HALVES * C])
        xw = sb("xw", [128, ZW])
        gates = sb("gates", [128, GATES * KB + KB])
        pair = sb("pair", [128, 2 * KB])
        h_first = sb("h_first", [128, KB])
        h_chunk = sb("h_chunk", [128, HALVES, STEPS, BATCH])
        h_half = sb("h_half", [128, HALVES * C])
        y_new = sb("y_new", [128, HALVES * C])
        y_old = sb("y_old", [128, HALVES * C])
        wy = sb("wy", [128, HALVES, STEPS, BATCH])
        rec = sb("rec", [128, HALVES, C])
        drive = sb("drive", [128, KB])
        decay = sb("decay", [128, KB])
        u = sb("u", [128, KB])
        spikes = sb("spikes", [128, HALVES, STEPS, BATCH])
        out_unit = sb("out_unit", [128, HALVES * C])
        out_row = sb("out_row", [128, HALVES * C])

        z_ps = [bank("z_ps0"), bank("z_ps1")]
        zt_ps = bank("zt_ps")
        xw_ps, wy_ps, rec_ps = bank("xw_ps"), bank("wy_ps"), bank("rec_ps")
        c_ps = bank("c_ps")
        c_new, c_tanh = c_ps[:, 0:KB], c_ps[:, KB:2 * KB]

        weights_in = sem("weights_in")
        setup = sem("setup")
        setup_done = sem("setup_done")
        x_in = sem("x_in")
        x_turned = sem("x_turned")
        x_kept = sem("x_kept")
        xw_summed = sem("xw_summed")
        xw_free = sem("xw_free")
        xw_ready = sem("xw_ready")
        z_ready = sem("z_ready")
        zt_ready = sem("zt_ready")
        gates_ready = sem("gates_ready")
        pair_ready = sem("pair_ready")
        c_ready = sem("c_ready")
        c_kept = sem("c_kept")
        tanh_ready = sem("tanh_ready")
        h_ready = sem("h_ready")
        h_halved = sem("h_halved")
        y_ready = sem("y_ready")
        y_kept = sem("y_kept")
        wy_summed = sem("wy_summed")
        wy_ready = sem("wy_ready")
        rec_summed = sem("rec_summed")
        rec_ready = sem("rec_ready")
        decay_ready = sem("decay_ready")
        drive_ready = sem("drive_ready")
        u_ready = sem("u_ready")
        s_ready = sem("s_ready")
        out_summed = sem("out_summed")
        out_ready = sem("out_ready")
        out_stored = sem("out_stored")

        def cols(w, k, j, n):
            return w[:, k, j, :] if len(w.shape) == 4 else w[:, k, j * n:(j + 1) * n]

        def product(ps, rows, left, w, n, start):
            for k in range(HALVES):
                for j in range(GROUPS):
                    last = nc.tensor.matmul(ps[C * j:C * j + rows, 0:n], left(k), cols(w, k, j, n),
                                            start=start and k == 0, stop=k == HALVES - 1,
                                            skip_group_check=True)
            return last

        def pe_chunk(pe, lstm, spiking, more, t0):
            for s in range(STEPS):
                t = t0 + s
                if lstm:
                    pe.wait_ge(h_ready, t + 1)
                    h = h_first if isinstance(t, int) and t == 0 else None
                    prev = (s - 1) % STEPS
                    left = (lambda k: h_first[:, BATCH * k:BATCH * (k + 1)]) if h is not None else \
                        (lambda k: h_chunk[:, k, prev, :])
                    product(z_ps[s % 2], BATCH, left, wh_sb, ZW, False).then_inc(z_ready, 1)
                if spiking:
                    vv = t - STEPS
                    pe.wait_ge(s_ready, vv + 1)
                    if isinstance(vv, int) and vv == 0:
                        left = lambda k: cond_sb[:, BATCH * k:BATCH * (k + 1)]
                    else:
                        prev_s = (s - 1) % STEPS
                        left = lambda k: spikes[:, k, prev_s, :]
                    product(rec_ps, BATCH, left, v_sb, HB, True).then_inc(rec_summed, 1)
                    if s == 0:
                        pe.wait_ge(y_ready, t)
                        product(wy_ps, C, lambda k: y_new[:, C * k:C * (k + 1)], wt_sb, HB,
                                True).then_inc(wy_summed, STEPS)
                if lstm and more and s == XT_SLOT:
                    pe.wait_ge(x_turned, t0 + 2 * STEPS)
                    product(xw_ps, C, lambda k: xt_next[:, C * k:C * (k + 1)], wx_sb, ZW,
                            True).then_inc(xw_summed, STEPS)
                if lstm and (more or s < STEPS - 1):
                    if s == STEPS - 1:
                        pe.wait_ge(xw_ready, t0 + 2 * STEPS)
                    last = pe_pick(s + 1)
                    if s == STEPS - 2:
                        last.then_inc(xw_free, STEPS)

        def pe_pick(s):
            row = BATCH * (s % STEPS)
            for j in range(GROUPS):
                last = nc.tensor.matmul(z_ps[s % 2][C * j:C * j + BATCH, 0:ZW],
                                        ident_sb[:, C * j + row:C * j + row + BATCH], xw[:, :],
                                        start=True, stop=False, skip_group_check=True)
            return last

        def dve_spike(dve, s, vv):
            dve.wait_ge(rec_summed, vv + 1)
            nc.vector.transpose(rec[:, :, :].rearrange("p k c -> p (k c)"),
                                rec_ps[:, 0:HALVES * C]).then_inc(rec_ready, 1)
            dve.wait_ge(drive_ready, vv + 1)
            dve.wait_ge(rec_ready, vv + 1)
            nc.vector.tensor_tensor(u[:, :].rearrange("p (k b) -> p k b", b=BATCH), rec[:, :, 0:BATCH],
                                    drive[:, :].rearrange("p (k b) -> p k b", b=BATCH),
                                    ALU.add).then_inc(u_ready, 1)
            dve.wait_ge(u_ready, vv + 2)
            nc.vector.tensor_scalar(spikes[:, :, s, :], u[:, :].rearrange("p (k b) -> p k b", b=BATCH),
                                    THRESHOLD, None, ALU.is_gt).then_inc(s_ready, 1)

        def dve_out(dve, step):
            dve.wait_ge(out_summed, step)
            nc.vector.transpose(out_row[:, :], out_unit[:, :]).then_inc(out_ready, STEPS)

        def dve_xw(dve, step):
            dve.wait_ge(xw_summed, step)
            nc.vector.tensor_tensor(xw[:, :], xw_ps[:, 0:ZW], bias_sb[:, :],
                                    ALU.add).then_inc(xw_ready, STEPS)

        def dve_turn_x(dve, step):
            dve.wait_ge(x_in, step)
            nc.vector.transpose(xt_next[:, :], x_row[:, :]).then_inc(x_turned, STEPS)

        def dve_lstm(dve, s, t):
            dve.wait_ge(z_ready, t + 1)
            nc.vector.transpose(zt_ps[:, 0:ZW], z_ps[s % 2][:, 0:ZW]).then_inc(zt_ready, 1)
            dve.wait_ge(c_kept, t + 1)
            dve.wait_ge(gates_ready, t + 1)
            nc.vector.scalar_tensor_tensor(out=pair[:, :], in0=gates[:, 0:2 * KB], scalar=1.0,
                                           in1=gates[:, 3 * KB:5 * KB], op0=ALU.add,
                                           op1=ALU.mult).then_inc(pair_ready, 1)
            dve.wait_ge(pair_ready, t + 1)
            for c_out, signal in ((c_new, c_ready), (gates[:, 4 * KB:5 * KB], c_kept)):
                nc.vector.scalar_tensor_tensor(out=c_out, in0=pair[:, KB:2 * KB], scalar=0.5,
                                               in1=pair[:, 0:KB], op0=ALU.mult,
                                               op1=ALU.add).then_inc(signal, 1)
            dve.wait_ge(tanh_ready, t + 1)
            nc.vector.scalar_tensor_tensor(
                out=h_chunk[:, :, s, :],
                in0=gates[:, 2 * KB:3 * KB].rearrange("p (k b) -> p k b", b=BATCH), scalar=1.0,
                in1=c_tanh.rearrange("p (k b) -> p k b", b=BATCH), op0=ALU.add,
                op1=ALU.mult).then_inc(h_ready, 1)

        def dve_chunk(dve, lstm, spiking, ending, more, t0, ready=None):
            for s in range(STEPS):
                t = t0 + s
                if spiking and s == 1:
                    dve.wait_ge(wy_summed, t0)
                    nc.vector.transpose(wy[:, :, :, :].rearrange("p k s b -> p (k s b)"),
                                        wy_ps[:, 0:HALVES * C]).then_inc(wy_ready, STEPS)
                    if ending:
                        dve.wait_ge(out_summed, t0 - STEPS)
                if (spiking and s > 0) or ending:
                    dve_spike(dve, (s - 1) % STEPS, t - STEPS - 1)
                if ending and s == 1:
                    if ready is not None:
                        dve.wait_ge(out_stored, ready)
                    dve_out(dve, t0 - STEPS)
                ending = ending and s < 1
                if lstm and more and s == XRAW_SLOT:
                    dve.wait_ge(x_kept, t0 + STEPS)
                    dve_turn_x(dve, t0 + 2 * STEPS)
                if lstm and more and s == STEPS - 1:
                    dve.wait_ge(xw_free, t0 + STEPS)
                    dve_xw(dve, t0 + 2 * STEPS)
                if lstm:
                    if s == 0 and spiking:
                        dve.wait_ge(h_halved, t0)
                    dve_lstm(dve, s, t)

        def act_chunk(act, t0):
            for s in range(STEPS):
                t = t0 + s
                act.wait_ge(zt_ready, t + 1)
                rows = zt_ps[:, 0:ZW].rearrange("p (m r) -> p m r", r=C)[:, :, 0:BATCH]
                nc.scalar.activation(gates[:, 0:GATES * KB].rearrange("p (m b) -> p m b", b=BATCH),
                                     rows, ACT.Tanh).then_inc(gates_ready, 1)
                act.wait_ge(c_ready, t + 1)
                nc.scalar.activation(c_tanh, c_new, ACT.Tanh, scale=0.5).then_inc(tanh_ready, 1)

        def pool_drive(pool, s, vv):
            pool.wait_ge(u_ready, vv + 1)
            nc.gpsimd.tensor_tensor(decay[:, :], u[:, :], a_unit[:, :], ALU.mult).then_inc(decay_ready, 1)
            pool.wait_ge(decay_ready, vv + 1)
            nc.gpsimd.tensor_tensor(drive[:, :].rearrange("p (k b) -> p k b", b=BATCH),
                                    decay[:, :].rearrange("p (k b) -> p k b", b=BATCH),
                                    wy[:, :, s, :], ALU.add).then_inc(drive_ready, 1)

        def pool_out(pool, step):
            pool.wait_ge(s_ready, step + 1)
            nc.gpsimd.tensor_tensor(out_unit[:, :], y_old[:, :],
                                    spikes[:, :, :, :].rearrange("p k s b -> p (k s b)"),
                                    ALU.add).then_inc(out_summed, STEPS)

        def pool_keep_x(pool, t0):
            pool.wait_ge(x_turned, t0 + STEPS)
            nc.gpsimd.tensor_copy(xt_now[:, :], xt_next[:, :]).then_inc(x_kept, STEPS)

        def pool_chunk(pool, lstm, ending, t0):
            pool.wait_ge(h_ready, t0 + 1)
            nc.gpsimd.tensor_scalar(h_half[:, :], h_chunk[:, :, :, :].rearrange("p k s b -> p (k s b)"),
                                    0.5, None, ALU.mult).then_inc(h_halved, STEPS)
            pool.wait_ge(h_halved, t0)
            nc.gpsimd.tensor_tensor(y_new[:, :], h_half[:, :], xt_now[:, :], ALU.add).then_inc(y_ready, STEPS)
            pool.wait_ge(y_ready, t0)
            if lstm:
                pool_keep_x(pool, t0)
            if ending:
                pool_out(pool, t0 - STEPS)
                pool.wait_ge(out_summed, t0 - STEPS)
            nc.gpsimd.tensor_copy(y_old[:, :], y_new[:, :]).then_inc(y_kept, STEPS)
            pool.wait_ge(wy_ready, t0)
            for s in range(STEPS):
                pool_drive(pool, s, t0 - STEPS + s)

        block = ctx.enter_context(nc.Block())

        @block.sync
        def _(sp):
            x_of = x.rearrange("(m p) n -> m p n", p=128)
            out_of = out.rearrange("(m p) n -> m p n", p=128)

            def load_x(m):
                sp.dma_start(x_row[:, :], x_of[m]).then_inc(x_in, 16)

            loads = ((wx_sb, wx), (wh_sb, wh), (wt_sb, wt), (v_sb, v))
            load_x(0)
            for dst, src in loads:
                sp.dma_start(dst[:], src.rearrange(
                    "p (k j n) -> p k j n", k=HALVES, j=GROUPS) if len(dst.shape) == 4 else
                    src.rearrange("p (k n) -> p k n", k=HALVES)).then_inc(weights_in, 16)
            for m in (1, 2):
                sp.wait_ge(x_turned, STEPS * m)
                load_x(m)
            with sp.Fori(2, CHUNKS - 1) as m:
                sp.wait_ge(out_ready, (m - 1) * STEPS)
                sp.dma_start(out_of[m - 2], out_row[:, :]).then_inc(out_stored, 16)
                sp.wait_ge(x_turned, (m + 1) * STEPS)
                load_x(m + 1)
            for m in range(CHUNKS - 3, CHUNKS):
                sp.wait_ge(out_ready, STEPS * (m + 1))
                sp.dma_start(out_of[m], out_row[:, :]).then_inc(out_stored, 16)
            sp.wait_ge(out_stored, 16 * CHUNKS)

        @block.gpsimd
        def _(pool):
            pool_keep_x(pool, 0)
            pool.wait_ge(x_kept, STEPS)
            pool_chunk(pool, True, False, STEPS)
            with pool.Fori(2 * STEPS, TIME, STEPS) as t0:
                pool_chunk(pool, True, True, t0)
            pool_chunk(pool, False, True, TIME)
            pool_out(pool, TIME)

        @block.scalar
        def _(act):
            for dst, src in ((bias_sb, bias), (ident_sb, ident), (eye_sb, eye), (noteye_sb, noteye),
                             (a_row, alpha_row), (a_raw, alpha_unit), (cond_sb, cond)):
                if dst is bias_sb:
                    for j in range(GROUPS):
                        act.dma_start(dst[C * j:C * (j + 1), :],
                                      src[j:j + 1, :].to_broadcast([C, ZW])).then_inc(weights_in, 16)
                elif dst is a_row:
                    act.dma_start(dst[:, :], src.to_broadcast([128, HID])).then_inc(weights_in, 16)
                elif len(dst.shape) == 3:
                    act.dma_start(dst[:], src.rearrange("p (k n) -> p k n", k=HALVES)).then_inc(weights_in, 16)
                else:
                    act.dma_start(dst[:, :], src).then_inc(weights_in, 16)
            act_chunk(act, 0)
            act_chunk(act, STEPS)
            with act.Fori(2 * STEPS, TIME, STEPS) as t0:
                act_chunk(act, t0)

        @block.vector
        def _(dve):
            n = 0
            for ps in (z_ps[0], z_ps[1], rec_ps):
                nc.vector.memset(ps[:, :], 0.0).then_inc(setup, 1)
                n += 1
            nc.vector.memset(gates[:, 4 * KB:5 * KB], 0.0).then_inc(c_kept, 1)
            dve_turn_x(dve, STEPS)
            dve.wait_ge(weights_in, 16 * 14)
            sig = 3 * HB
            for w, f_sig, f_tanh in ((wx_sb, 0.5, None), (bias_sb, 0.5, None), (wh_sb, 0.25, 0.5)):
                w3 = w[:, :, :, :].rearrange("p k j n -> p (k j) n") if len(w.shape) == 4 else w[:, :]
                part = (lambda a, b: w3[:, :, a:b]) if len(w.shape) == 4 else (lambda a, b: w3[:, a:b])
                nc.vector.tensor_scalar(part(0, sig), part(0, sig), f_sig, None, ALU.mult).then_inc(setup, 1)
                n += 1
                if f_tanh is not None:
                    nc.vector.tensor_scalar(part(sig, ZW), part(sig, ZW), f_tanh, None,
                                            ALU.mult).then_inc(setup, 1)
                    n += 1
            nc.vector.tensor_scalar(h_first[:, :], cond_sb[:, :], 2.0, None, ALU.mult).then_inc(setup, 1)
            nc.vector.tensor_copy(u[:, :], cond_sb[:, :]).then_inc(setup, 1)
            nc.vector.tensor_scalar(a_row[:, :], a_row[:, :], ALPHA_LO, ALPHA_HI, ALU.max,
                                    ALU.min).then_inc(setup, 1)
            nc.vector.tensor_scalar(
                a_unit[:, :].rearrange("p (k b) -> p k b", b=BATCH),
                a_raw[:, :].unsqueeze(2).to_broadcast([128, HALVES, BATCH]), ALPHA_LO, ALPHA_HI,
                ALU.max, ALU.min).then_inc(setup, 1)
            n += 4
            dve.wait_ge(setup, n)
            nc.vector.sem_inc(setup_done, 1)
            dve_xw(dve, STEPS)
            nc.vector.tensor_scalar(oma_row[:, :], a_row[:, :], -1.0, 1.0, ALU.mult, ALU.add).then_inc(setup, 1)
            nc.vector.tensor_tensor(v_sb[:], v_sb[:], noteye_sb[:], ALU.mult).then_inc(setup, 1)
            n += 2
            dve.wait_ge(setup, n)
            for k in range(HALVES):
                nc.vector.tensor_tensor(wt_sb[:, k, :], wt_sb[:, k, :], oma_row[:, :], ALU.mult).then_inc(setup, 1)
                nc.vector.tensor_tensor(v_sb[:, k, :], v_sb[:, k, :], oma_row[:, :], ALU.mult).then_inc(setup, 1)
                nc.vector.tensor_tensor(eye_sb[:, k, :], eye_sb[:, k, :], a_row[:, :], ALU.mult).then_inc(setup, 1)
                n += 3
            dve.wait_ge(setup, n)
            nc.vector.tensor_tensor(v_sb[:], v_sb[:], eye_sb[:], ALU.subtract).then_inc(setup, 1)
            dve.wait_ge(setup, n + 1)
            for signal in (h_ready, u_ready, s_ready):
                nc.vector.sem_inc(signal, 1)
            dve_chunk(dve, True, False, False, True, 0)
            dve_chunk(dve, True, True, False, True, STEPS)
            with dve.Fori(2 * STEPS, TIME - STEPS, STEPS) as t0:
                dve_chunk(dve, True, True, True, True, t0, t0 - 2 * STEPS)
            dve_chunk(dve, True, True, True, False, TIME - STEPS, TIME - 3 * STEPS)
            dve_chunk(dve, False, True, True, False, TIME, TIME - 2 * STEPS)
            dve_spike(dve, STEPS - 1, TIME - 1)
            dve.wait_ge(out_stored, TIME - STEPS)
            dve_out(dve, TIME)

        @block.tensor
        def _(pe):
            pe.wait_ge(setup_done, 1)
            pe.wait_ge(x_turned, STEPS)
            product(xw_ps, C, lambda k: xt_next[:, C * k:C * (k + 1)], wx_sb, ZW,
                    True).then_inc(xw_summed, STEPS)
            pe.wait_ge(xw_ready, STEPS)
            pe_pick(0)
            pe_chunk(pe, True, False, True, 0)
            pe_chunk(pe, True, True, True, STEPS)
            with pe.Fori(2 * STEPS, TIME - STEPS, STEPS) as t0:
                pe_chunk(pe, True, True, True, t0)
            pe_chunk(pe, True, True, False, TIME - STEPS)
            pe_chunk(pe, False, True, False, TIME)


def kernel(x, cond_1024, L0_cond_Wx, L0_cond_Wh, L0_cond_b, L1_cond_W, L1_cond_V, L1_cond_alpha):
    import concourse.bacc as bacc
    from concourse.bass_utils import run_bass_kernel_spmd

    def units(a):
        return a.reshape(GROUPS, HALVES, C, -1).transpose(0, 2, 1, 3).reshape(128, -1)

    def lstm_weights(w):
        return units(w.reshape(-1, GATES, GROUPS, HB).transpose(0, 2, 1, 3).reshape(HID, GROUPS * ZW))

    x, cond, wx, wh, b, w, v, alpha = (np.asarray(a) for a in (
        x, cond_1024, L0_cond_Wx, L0_cond_Wh, L0_cond_b, L1_cond_W, L1_cond_V, L1_cond_alpha))
    eye = np.eye(HID, dtype=np.float32)
    arrays = {
        "x": x.reshape(BATCH, CHUNKS, STEPS, GROUPS, HB).transpose(1, 3, 2, 0, 4).reshape(CHUNKS * 128, HB),
        "cond": units(cond.T),
        "wx": lstm_weights(wx),
        "wh": lstm_weights(wh),
        "bias": b.reshape(GATES, GROUPS, HB).transpose(1, 0, 2).reshape(GROUPS, ZW),
        "wt": units(w.T),
        "v": units(v),
        "eye": units(eye),
        "noteye": units(1.0 - eye),
        "ident": np.eye(128, dtype=np.float32),
        "alpha_row": alpha.reshape(1, HID),
        "alpha_unit": units(alpha.reshape(HID, 1)),
    }
    arrays = {name: np.ascontiguousarray(a) for name, a in arrays.items()}
    nc = bacc.Bacc("TRN2", target_bir_lowering=False, num_devices=1)
    args = {name: nc.dram_tensor(name, a.shape, F32, kind="ExternalInput").ap() for name, a in arrays.items()}
    out = nc.dram_tensor("out", (CHUNKS * 128, HB), F32, kind="ExternalOutput").ap()
    build(nc, out=out, **args)
    result = run_bass_kernel_spmd(nc, [arrays], core_ids=[0]).results[0]["out"]
    return result.reshape(CHUNKS, GROUPS, STEPS, BATCH, HB).transpose(3, 0, 2, 1, 4).reshape(BATCH, TIME, HID)
```

```python
from contextlib import ExitStack

import numpy as np

import concourse.bass as bass
import concourse.mybir as mybir

F32 = mybir.dt.float32
ALU = mybir.AluOpType
ACT = mybir.ActivationFunctionType

BATCH, TIME, HID = 2, 1024, 256
C = 32
GROUPS = 4
HB = HID // GROUPS
HALVES = HB // C
GATES = 4
ORDER = [0, 1, 3, 2]
ZW = GATES * HB
CW = 3 * HB
STEPS = C // BATCH
CHUNKS = TIME // STEPS
assert STEPS == 16
KB = HALVES * BATCH
ALPHA_LO = float(np.exp(-1.0 / 5.0))
ALPHA_HI = float(np.exp(-1.0 / 25.0))
THRESHOLD = 1.0
XRAW_SLOT, XT_SLOT = 8, 12


def build(nc, x, cond, wx, wh, bias, wt, v, eye, noteye, ident, alpha_row, alpha_unit, out):
    with ExitStack() as ctx:
        def sb(name, shape):
            return ctx.enter_context(nc.sbuf_tensor(name, shape, F32))

        def bank(name):
            return ctx.enter_context(nc.psum_tensor(name, [128, 512], F32))

        def sem(name):
            return ctx.enter_context(nc.semaphore(name))

        wx_sb = sb("wx_sb", [128, HALVES, GROUPS, ZW])
        wh_sb = sb("wh_sb", [128, HALVES, GROUPS, ZW])
        bias_sb = sb("bias_sb", [128, ZW])
        wt_sb = sb("wt_sb", [128, HALVES, GROUPS, HB])
        v_sb = sb("v_sb", [128, HALVES, GROUPS, HB])
        eye_sb = sb("eye_sb", [128, HALVES, GROUPS, HB])
        noteye_sb = sb("noteye_sb", [128, HALVES, GROUPS, HB])
        ident_sb = sb("ident_sb", [128, 128])
        a_row = sb("a_row", [128, GROUPS, HB])
        oma_row = sb("oma_row", [128, GROUPS, HB])
        a_raw = sb("a_raw", [128, HALVES])
        a_unit = sb("a_unit", [128, KB])
        cond_sb = sb("cond_sb", [128, KB])
        x_row = sb("x_row", [128, HB])
        xt_next = sb("xt_next", [128, HALVES * C])
        xt_now = sb("xt_now", [128, HALVES * C])
        xw = sb("xw", [128, ZW])
        gates = sb("gates", [128, 4 * KB])
        gate_o = sb("gate_o", [128, KB])
        ot = sb("ot", [128, HALVES, C])
        pair = sb("pair", [128, 2 * KB])
        h_first = sb("h_first", [128, KB])
        h_chunk = sb("h_chunk", [128, HALVES, STEPS, BATCH])
        h_half = sb("h_half", [128, HALVES * C])
        y_new = sb("y_new", [128, HALVES * C])
        y_old = sb("y_old", [128, HALVES * C])
        wy = sb("wy", [128, HALVES, STEPS, BATCH])
        rec = sb("rec", [128, HALVES, C])
        drive = sb("drive", [128, KB])
        decay = sb("decay", [128, KB])
        u = sb("u", [128, KB])
        spikes = sb("spikes", [128, HALVES, STEPS, BATCH])
        out_unit = sb("out_unit", [128, HALVES * C])
        out_row = sb("out_row", [128, HALVES * C])

        z_ps = [bank("z_ps0"), bank("z_ps1")]
        o_ps = [bank("o_ps0"), bank("o_ps1")]
        unit_ps = bank("unit_ps")
        zt_ps = unit_ps[:, 0:CW]
        xw_ps, wy_ps, rec_ps = bank("xw_ps"), bank("wy_ps"), bank("rec_ps")
        c_new, c_tanh = unit_ps[:, CW:CW + KB], unit_ps[:, CW + KB:CW + 2 * KB]

        weights_in = sem("weights_in")
        setup = sem("setup")
        setup_done = sem("setup_done")
        x_in = sem("x_in")
        x_turned = sem("x_turned")
        x_kept = sem("x_kept")
        xw_summed = sem("xw_summed")
        xw_free = sem("xw_free")
        xw_ready = sem("xw_ready")
        z_ready = sem("z_ready")
        zt_ready = sem("zt_ready")
        o_summed = sem("o_summed")
        ot_ready = sem("ot_ready")
        gates_ready = sem("gates_ready")
        pair_ready = sem("pair_ready")
        c_ready = sem("c_ready")
        c_kept = sem("c_kept")
        tanh_ready = sem("tanh_ready")
        h_ready = sem("h_ready")
        h_halved = sem("h_halved")
        y_ready = sem("y_ready")
        y_kept = sem("y_kept")
        wy_summed = sem("wy_summed")
        wy_ready = sem("wy_ready")
        rec_summed = sem("rec_summed")
        rec_ready = sem("rec_ready")
        decay_ready = sem("decay_ready")
        drive_ready = sem("drive_ready")
        u_ready = sem("u_ready")
        s_ready = sem("s_ready")
        out_summed = sem("out_summed")
        out_ready = sem("out_ready")
        out_stored = sem("out_stored")

        def product(ps, rows, left, w, start, lo=0, hi=HB):
            for k in range(HALVES):
                for j in range(GROUPS):
                    last = nc.tensor.matmul(ps[C * j:C * j + rows, 0:hi - lo], left(k), w[:, k, j, lo:hi],
                                            start=start and k == 0, stop=k == HALVES - 1,
                                            skip_group_check=True)
            return last

        def pe_chunk(pe, lstm, spiking, more, t0):
            for s in range(STEPS):
                t = t0 + s
                if lstm:
                    pe.wait_ge(h_ready, t + 1)
                    h = h_first if isinstance(t, int) and t == 0 else None
                    prev = (s - 1) % STEPS
                    left = (lambda k: h_first[:, BATCH * k:BATCH * (k + 1)]) if h is not None else \
                        (lambda k: h_chunk[:, k, prev, :])
                    product(z_ps[s % 2], BATCH, left, wh_sb, False, 0, CW).then_inc(z_ready, 1)
                    product(o_ps[s % 2], BATCH, left, wh_sb, False, CW, ZW).then_inc(o_summed, 1)
                if spiking:
                    vv = t - STEPS
                    pe.wait_ge(s_ready, vv + 1)
                    if isinstance(vv, int) and vv == 0:
                        left = lambda k: cond_sb[:, BATCH * k:BATCH * (k + 1)]
                    else:
                        prev_s = (s - 1) % STEPS
                        left = lambda k: spikes[:, k, prev_s, :]
                    product(rec_ps, BATCH, left, v_sb, True).then_inc(rec_summed, 1)
                    if s == 0:
                        pe.wait_ge(y_ready, t)
                        product(wy_ps, C, lambda k: y_new[:, C * k:C * (k + 1)], wt_sb,
                                True).then_inc(wy_summed, STEPS)
                if lstm and more and s == XT_SLOT:
                    pe.wait_ge(x_turned, t0 + 2 * STEPS)
                    product(xw_ps, C, lambda k: xt_next[:, C * k:C * (k + 1)], wx_sb,
                            True, 0, ZW).then_inc(xw_summed, STEPS)
                if lstm and (more or s < STEPS - 1):
                    if s == STEPS - 1:
                        pe.wait_ge(xw_ready, t0 + 2 * STEPS)
                    last = pe_pick(s + 1)
                    if s == STEPS - 2:
                        last.then_inc(xw_free, STEPS)

        def pe_pick(s):
            row = BATCH * (s % STEPS)
            for ps, lo, hi in ((z_ps[s % 2], 0, CW), (o_ps[s % 2], CW, ZW)):
                for j in range(GROUPS):
                    last = nc.tensor.matmul(ps[C * j:C * j + BATCH, 0:hi - lo],
                                            ident_sb[:, C * j + row:C * j + row + BATCH], xw[:, lo:hi],
                                            start=True, stop=False, skip_group_check=True)
            return last

        def dve_spike(dve, s, vv):
            dve.wait_ge(rec_summed, vv + 1)
            nc.vector.transpose(rec[:, :, :].rearrange("p k c -> p (k c)"),
                                rec_ps[:, 0:HALVES * C]).then_inc(rec_ready, 1)
            dve.wait_ge(drive_ready, vv + 1)
            dve.wait_ge(rec_ready, vv + 1)
            nc.vector.tensor_tensor(u[:, :].rearrange("p (k b) -> p k b", b=BATCH), rec[:, :, 0:BATCH],
                                    drive[:, :].rearrange("p (k b) -> p k b", b=BATCH),
                                    ALU.add).then_inc(u_ready, 1)
            dve.wait_ge(u_ready, vv + 2)
            nc.vector.tensor_scalar(spikes[:, :, s, :], u[:, :].rearrange("p (k b) -> p k b", b=BATCH),
                                    THRESHOLD, None, ALU.is_gt).then_inc(s_ready, 1)

        def dve_out(dve, step):
            dve.wait_ge(out_summed, step)
            nc.vector.transpose(out_row[:, :], out_unit[:, :]).then_inc(out_ready, STEPS)

        def dve_xw(dve, step):
            dve.wait_ge(xw_summed, step)
            nc.vector.tensor_tensor(xw[:, :], xw_ps[:, 0:ZW], bias_sb[:, :],
                                    ALU.add).then_inc(xw_ready, STEPS)

        def dve_turn_x(dve, step):
            dve.wait_ge(x_in, step)
            nc.vector.transpose(xt_next[:, :], x_row[:, :]).then_inc(x_turned, STEPS)

        def dve_lstm(dve, s, t):
            dve.wait_ge(z_ready, t + 1)
            nc.vector.transpose(zt_ps, z_ps[s % 2][:, 0:CW]).then_inc(zt_ready, 1)
            dve.wait_ge(o_summed, t + 1)
            nc.vector.transpose(ot[:, :, :].rearrange("p k c -> p (k c)"), o_ps[s % 2][:, 0:HB]).then_inc(ot_ready, 1)
            dve.wait_ge(gates_ready, t + 1)
            nc.vector.scalar_tensor_tensor(out=pair[:, :], in0=gates[:, 0:2 * KB], scalar=1.0,
                                           in1=gates[:, 2 * KB:4 * KB], op0=ALU.add,
                                           op1=ALU.mult).then_inc(pair_ready, 1)
            dve.wait_ge(pair_ready, t + 1)
            for c_out, signal in ((c_new, c_ready), (gates[:, 3 * KB:4 * KB], c_kept)):
                nc.vector.scalar_tensor_tensor(out=c_out, in0=pair[:, KB:2 * KB], scalar=0.5,
                                               in1=pair[:, 0:KB], op0=ALU.mult,
                                               op1=ALU.add).then_inc(signal, 1)
            dve.wait_ge(tanh_ready, t + 1)
            nc.vector.scalar_tensor_tensor(
                out=h_chunk[:, :, s, :],
                in0=gate_o[:, :].rearrange("p (k b) -> p k b", b=BATCH), scalar=1.0,
                in1=c_tanh.rearrange("p (k b) -> p k b", b=BATCH), op0=ALU.add,
                op1=ALU.mult).then_inc(h_ready, 1)

        def dve_chunk(dve, lstm, spiking, ending, more, t0, ready=None):
            for s in range(STEPS):
                t = t0 + s
                if spiking and s == 1:
                    dve.wait_ge(wy_summed, t0)
                    nc.vector.transpose(wy[:, :, :, :].rearrange("p k s b -> p (k s b)"),
                                        wy_ps[:, 0:HALVES * C]).then_inc(wy_ready, STEPS)
                    if ending:
                        dve.wait_ge(out_summed, t0 - STEPS)
                if lstm:
                    dve.wait_ge(c_kept, t + 1)
                if (spiking and s > 0) or ending:
                    dve_spike(dve, (s - 1) % STEPS, t - STEPS - 1)
                if ending and s == 1:
                    if ready is not None:
                        dve.wait_ge(out_stored, ready)
                    dve_out(dve, t0 - STEPS)
                ending = ending and s < 1
                if lstm and more and s == XRAW_SLOT:
                    dve.wait_ge(x_kept, t0 + STEPS)
                    dve_turn_x(dve, t0 + 2 * STEPS)
                if lstm and more and s == STEPS - 1:
                    dve.wait_ge(xw_free, t0 + STEPS)
                    dve_xw(dve, t0 + 2 * STEPS)
                if lstm:
                    if s == 0 and spiking:
                        dve.wait_ge(h_halved, t0)
                    dve_lstm(dve, s, t)

        def act_chunk(act, t0):
            for s in range(STEPS):
                t = t0 + s
                act.wait_ge(zt_ready, t + 1)
                rows = zt_ps.rearrange("p (m r) -> p m r", r=C)[:, :, 0:BATCH]
                nc.scalar.activation(gates[:, 0:3 * KB].rearrange("p (m b) -> p m b", b=BATCH),
                                     rows, ACT.Tanh).then_inc(gates_ready, 1)
                act.wait_ge(ot_ready, t + 1)
                nc.scalar.activation(gate_o[:, :].rearrange("p (k b) -> p k b", b=BATCH),
                                     ot[:, :, 0:BATCH], ACT.Tanh)
                act.wait_ge(c_ready, t + 1)
                nc.scalar.activation(c_tanh, c_new, ACT.Tanh, scale=0.5).then_inc(tanh_ready, 1)

        def pool_drive(pool, s, vv):
            pool.wait_ge(u_ready, vv + 1)
            nc.gpsimd.tensor_tensor(decay[:, :], u[:, :], a_unit[:, :], ALU.mult).then_inc(decay_ready, 1)
            if s == 0:
                pool.wait_ge(wy_ready, vv + STEPS)
            pool.wait_ge(decay_ready, vv + 1)
            nc.gpsimd.tensor_tensor(drive[:, :].rearrange("p (k b) -> p k b", b=BATCH),
                                    decay[:, :].rearrange("p (k b) -> p k b", b=BATCH),
                                    wy[:, :, s, :], ALU.add).then_inc(drive_ready, 1)

        def pool_out(pool, step):
            pool.wait_ge(s_ready, step + 1)
            nc.gpsimd.tensor_tensor(out_unit[:, :], y_old[:, :],
                                    spikes[:, :, :, :].rearrange("p k s b -> p (k s b)"),
                                    ALU.add).then_inc(out_summed, STEPS)

        def pool_keep_x(pool, t0):
            pool.wait_ge(x_turned, t0 + STEPS)
            nc.gpsimd.tensor_copy(xt_now[:, :], xt_next[:, :]).then_inc(x_kept, STEPS)

        def pool_chunk(pool, lstm, ending, t0):
            pool.wait_ge(h_ready, t0 + 1)
            nc.gpsimd.tensor_scalar(h_half[:, :], h_chunk[:, :, :, :].rearrange("p k s b -> p (k s b)"),
                                    0.5, None, ALU.mult).then_inc(h_halved, STEPS)
            pool.wait_ge(h_halved, t0)
            nc.gpsimd.tensor_tensor(y_new[:, :], h_half[:, :], xt_now[:, :], ALU.add).then_inc(y_ready, STEPS)
            pool.wait_ge(y_ready, t0)
            if lstm:
                pool_keep_x(pool, t0)
            if ending:
                pool_out(pool, t0 - STEPS)
                pool.wait_ge(out_summed, t0 - STEPS)
            nc.gpsimd.tensor_copy(y_old[:, :], y_new[:, :]).then_inc(y_kept, STEPS)
            for s in range(STEPS):
                pool_drive(pool, s, t0 - STEPS + s)

        block = ctx.enter_context(nc.Block())

        @block.sync
        def _(sp):
            x_of = x.rearrange("(m p) n -> m p n", p=128)
            out_of = out.rearrange("(m p) n -> m p n", p=128)

            def load_x(m):
                sp.dma_start(x_row[:, :], x_of[m]).then_inc(x_in, 16)

            loads = ((wx_sb, wx), (wh_sb, wh), (wt_sb, wt), (v_sb, v))
            load_x(0)
            for dst, src in loads:
                sp.dma_start(dst[:], src.rearrange("p (k j n) -> p k j n", k=HALVES,
                                                   j=GROUPS)).then_inc(weights_in, 16)
            for m in (1, 2):
                sp.wait_ge(x_turned, STEPS * m)
                load_x(m)
            with sp.Fori(2, CHUNKS - 1) as m:
                sp.wait_ge(out_ready, (m - 1) * STEPS)
                sp.dma_start(out_of[m - 2], out_row[:, :]).then_inc(out_stored, 16)
                sp.wait_ge(x_turned, (m + 1) * STEPS)
                load_x(m + 1)
            for m in range(CHUNKS - 3, CHUNKS):
                sp.wait_ge(out_ready, STEPS * (m + 1))
                sp.dma_start(out_of[m], out_row[:, :]).then_inc(out_stored, 16)
            sp.wait_ge(out_stored, 16 * CHUNKS)

        @block.gpsimd
        def _(pool):
            pool_keep_x(pool, 0)
            pool.wait_ge(x_kept, STEPS)
            pool_chunk(pool, True, False, STEPS)
            with pool.Fori(2 * STEPS, TIME, STEPS) as t0:
                pool_chunk(pool, True, True, t0)
            pool_chunk(pool, False, True, TIME)
            pool_out(pool, TIME)

        @block.scalar
        def _(act):
            for dst, src in ((bias_sb, bias), (ident_sb, ident), (eye_sb, eye), (noteye_sb, noteye),
                             (a_row, alpha_row), (a_raw, alpha_unit), (cond_sb, cond)):
                if dst is bias_sb:
                    for j in range(GROUPS):
                        act.dma_start(dst[C * j:C * (j + 1), :],
                                      src[j:j + 1, :].to_broadcast([C, ZW])).then_inc(weights_in, 16)
                elif dst is a_row:
                    act.dma_start(dst[:, :, :].rearrange("p j n -> p (j n)"),
                                  src.to_broadcast([128, HID])).then_inc(weights_in, 16)
                elif len(dst.shape) == 4:
                    act.dma_start(dst[:], src.rearrange("p (k j n) -> p k j n", k=HALVES,
                                                        j=GROUPS)).then_inc(weights_in, 16)
                else:
                    act.dma_start(dst[:, :], src).then_inc(weights_in, 16)
            act_chunk(act, 0)
            act_chunk(act, STEPS)
            with act.Fori(2 * STEPS, TIME, STEPS) as t0:
                act_chunk(act, t0)

        @block.vector
        def _(dve):
            n = 0
            for ps in (*z_ps, *o_ps, rec_ps):
                nc.vector.memset(ps[:, :], 0.0).then_inc(setup, 1)
                n += 1
            nc.vector.memset(gates[:, 3 * KB:4 * KB], 0.0).then_inc(c_kept, 1)
            dve_turn_x(dve, STEPS)
            dve.wait_ge(weights_in, 16 * 14)
            for w, f_sigmoid, f_tanh in ((bias_sb, 0.5, 1.0), (wx_sb, 0.5, 1.0), (wh_sb, 0.25, 0.5)):
                rows = w[:, :] if w is bias_sb else w[:, :, :, :].rearrange("p k j n -> p (k j) n")
                for lo, hi, f in ((0, 2 * HB, f_sigmoid), (2 * HB, CW, f_tanh), (CW, ZW, f_sigmoid)):
                    if f != 1.0:
                        part = rows[..., lo:hi]
                        nc.vector.tensor_scalar(part, part, f, None, ALU.mult).then_inc(setup, 1)
                        n += 1
            nc.vector.tensor_scalar(h_first[:, :], cond_sb[:, :], 2.0, None, ALU.mult).then_inc(setup, 1)
            nc.vector.tensor_copy(u[:, :], cond_sb[:, :]).then_inc(setup, 1)
            nc.vector.tensor_scalar(a_row[:], a_row[:], ALPHA_LO, ALPHA_HI, ALU.max,
                                    ALU.min).then_inc(setup, 1)
            nc.vector.tensor_scalar(
                a_unit[:, :].rearrange("p (k b) -> p k b", b=BATCH),
                a_raw[:, :].unsqueeze(2).to_broadcast([128, HALVES, BATCH]), ALPHA_LO, ALPHA_HI,
                ALU.max, ALU.min).then_inc(setup, 1)
            n += 4
            dve.wait_ge(setup, n)
            nc.vector.sem_inc(setup_done, 1)
            dve_xw(dve, STEPS)
            nc.vector.tensor_scalar(oma_row[:], a_row[:], -1.0, 1.0, ALU.mult, ALU.add).then_inc(setup, 1)
            nc.vector.tensor_tensor(v_sb[:], v_sb[:], noteye_sb[:], ALU.mult).then_inc(setup, 1)
            n += 2
            dve.wait_ge(setup, n)
            for k in range(HALVES):
                nc.vector.tensor_tensor(wt_sb[:, k], wt_sb[:, k], oma_row[:], ALU.mult).then_inc(setup, 1)
                nc.vector.tensor_tensor(v_sb[:, k], v_sb[:, k], oma_row[:], ALU.mult).then_inc(setup, 1)
                nc.vector.tensor_tensor(eye_sb[:, k], eye_sb[:, k], a_row[:], ALU.mult).then_inc(setup, 1)
                n += 3
            dve.wait_ge(setup, n)
            nc.vector.tensor_tensor(v_sb[:], v_sb[:], eye_sb[:], ALU.subtract).then_inc(setup, 1)
            dve.wait_ge(setup, n + 1)
            for signal in (h_ready, u_ready, s_ready):
                nc.vector.sem_inc(signal, 1)
            dve_chunk(dve, True, False, False, True, 0)
            dve_chunk(dve, True, True, False, True, STEPS)
            with dve.Fori(2 * STEPS, TIME - STEPS, STEPS) as t0:
                dve_chunk(dve, True, True, True, True, t0, t0 - 2 * STEPS)
            dve_chunk(dve, True, True, True, False, TIME - STEPS, TIME - 3 * STEPS)
            dve_chunk(dve, False, True, True, False, TIME, TIME - 2 * STEPS)
            dve_spike(dve, STEPS - 1, TIME - 1)
            dve.wait_ge(out_stored, TIME - STEPS)
            dve_out(dve, TIME)

        @block.tensor
        def _(pe):
            pe.wait_ge(setup_done, 1)
            pe.wait_ge(x_turned, STEPS)
            product(xw_ps, C, lambda k: xt_next[:, C * k:C * (k + 1)], wx_sb,
                    True, 0, ZW).then_inc(xw_summed, STEPS)
            pe.wait_ge(xw_ready, STEPS)
            pe_pick(0)
            pe_chunk(pe, True, False, True, 0)
            pe_chunk(pe, True, True, True, STEPS)
            with pe.Fori(2 * STEPS, TIME - STEPS, STEPS) as t0:
                pe_chunk(pe, True, True, True, t0)
            pe_chunk(pe, True, True, False, TIME - STEPS)
            pe_chunk(pe, False, True, False, TIME)


def kernel(x, cond_1024, L0_cond_Wx, L0_cond_Wh, L0_cond_b, L1_cond_W, L1_cond_V, L1_cond_alpha):
    import concourse.bacc as bacc
    from concourse.bass_utils import run_bass_kernel_spmd

    def units(a):
        return a.reshape(GROUPS, HALVES, C, -1).transpose(0, 2, 1, 3).reshape(128, -1)

    def lstm_weights(w):
        return units(w.reshape(HID, GATES, GROUPS, HB)[:, ORDER].transpose(0, 2, 1, 3).reshape(HID, -1))

    x, cond, wx, wh, b, w, v, alpha = (np.asarray(a) for a in (
        x, cond_1024, L0_cond_Wx, L0_cond_Wh, L0_cond_b, L1_cond_W, L1_cond_V, L1_cond_alpha))
    eye = np.eye(HID, dtype=np.float32)
    arrays = {
        "x": x.reshape(BATCH, CHUNKS, STEPS, GROUPS, HB).transpose(1, 3, 2, 0, 4).reshape(CHUNKS * 128, HB),
        "cond": units(cond.T),
        "wx": lstm_weights(wx),
        "wh": lstm_weights(wh),
        "bias": b.reshape(GATES, GROUPS, HB)[ORDER].transpose(1, 0, 2).reshape(GROUPS, ZW),
        "wt": units(w.T),
        "v": units(v),
        "eye": units(eye),
        "noteye": units(1.0 - eye),
        "ident": np.eye(128, dtype=np.float32),
        "alpha_row": alpha.reshape(1, HID),
        "alpha_unit": units(alpha.reshape(HID, 1)),
    }
    arrays = {name: np.ascontiguousarray(a) for name, a in arrays.items()}
    nc = bacc.Bacc("TRN2", target_bir_lowering=False, num_devices=1)
    args = {name: nc.dram_tensor(name, a.shape, F32, kind="ExternalInput").ap() for name, a in arrays.items()}
    out = nc.dram_tensor("out", (CHUNKS * 128, HB), F32, kind="ExternalOutput").ap()
    build(nc, out=out, **args)
    result = run_bass_kernel_spmd(nc, [arrays], core_ids=[0]).results[0]["out"]
    return result.reshape(CHUNKS, GROUPS, STEPS, BATCH, HB).transpose(3, 0, 2, 1, 4).reshape(BATCH, TIME, HID)
```

```python
from contextlib import ExitStack

import numpy as np

import concourse.bass as bass
import concourse.mybir as mybir

F32, BF16 = mybir.dt.float32, mybir.dt.bfloat16
ALU = mybir.AluOpType
ACT = mybir.ActivationFunctionType

BATCH, TIME, HID = 2, 1024, 256
C = 32
GROUPS = 4
HB = HID // GROUPS
HALVES = HB // C
GATES = 4
ORDER = [0, 3, 1, 2]
ZW = GATES * HB
IG, F, O = (0, 2 * HB), (2 * HB, 3 * HB), (3 * HB, ZW)
STEPS = C // BATCH
CHUNKS = TIME // STEPS
LOOP_END = TIME - 2 * STEPS
assert CHUNKS % 2 == 0
assert STEPS == 16
KB = HALVES * BATCH
ALPHA_LO = float(np.exp(-1.0 / 5.0))
ALPHA_HI = float(np.exp(-1.0 / 25.0))
THRESHOLD = 1.0
PARTS = 3
MOVES = PARTS * GROUPS
OUT_SLOT = 3
TURN_SLOT = 2
PRODUCT_SLOT = 3
PIECES = [(k, lo, lo + ZW // 2) for lo in (0, ZW // 2) for k in range(HALVES)]
SUM_SLOT = PRODUCT_SLOT + len(PIECES)
SPLIT_SLOT = SUM_SLOT + 2
SPLIT_COUNT = STEPS // (PARTS + 1)
SPLIT_DONE = (1, 3, 4)


def build(nc, x, cond, wx, wh, bias, wt, v, eye, noteye, select, alpha_row, alpha_unit, out):
    with ExitStack() as ctx:
        def sb(name, shape, dtype=F32):
            return ctx.enter_context(nc.sbuf_tensor(name, shape, dtype))

        def chunk_loop(engine, last):
            return nc.Fori(2 * STEPS, last, 2 * STEPS, engines=(engine,), hint_back_edge=True)

        def bank(name):
            return ctx.enter_context(nc.psum_tensor(name, [128, 512], F32))

        def sem(name):
            return ctx.enter_context(nc.semaphore(name))

        wx_sb = sb("wx_sb", [128, HALVES, GROUPS, ZW])
        wh_sb = sb("wh_sb", [128, HALVES, GROUPS, ZW])
        bias_sb = sb("bias_sb", [128, ZW])
        wt_sb = sb("wt_sb", [128, HALVES, GROUPS, HB])
        v_sb = sb("v_sb", [128, HALVES, GROUPS, HB])
        eye_sb = sb("eye_sb", [128, HALVES, GROUPS, HB])
        noteye_sb = sb("noteye_sb", [128, HALVES, GROUPS, HB])
        select_sb = sb("select_sb", [PARTS * C, C])
        select_bf = sb("select_bf", [PARTS * C, C], BF16)
        a_row = sb("a_row", [128, GROUPS, HB])
        oma_row = sb("oma_row", [128, GROUPS, HB])
        a_raw = sb("a_raw", [128, HALVES])
        a_unit = sb("a_unit", [128, KB])
        cond_sb = sb("cond_sb", [128, KB])
        x_row = sb("x_row", [128, HB])
        xt_next = sb("xt_next", [128, HALVES * C])
        xt_now = sb("xt_now", [128, HALVES * C])
        xw_sum = sb("xw_sum", [128, ZW])
        xw_rest = sb("xw_rest", [128, ZW])
        xw_parts = sb("xw_parts", [128, PARTS, ZW], BF16)
        xw_next = sb("xw_next", [PARTS * C, GROUPS, ZW], BF16)
        xw = sb("xw", [PARTS * C, GROUPS, ZW], BF16)
        gates_ig = sb("gates_ig", [128, 2, KB])
        gate_o = sb("gate_o", [128, KB])
        scan_mul = sb("scan_mul", [128, KB, 3])
        scan_add = sb("scan_add", [128, KB, 3])
        h_first = sb("h_first", [128, KB])
        h_chunk = sb("h_chunk", [128, HALVES, STEPS, BATCH])
        h_half = sb("h_half", [128, HALVES * C])
        y_new = sb("y_new", [128, HALVES * C])
        y_old = sb("y_old", [128, HALVES * C])
        wy = sb("wy", [128, HALVES, STEPS, BATCH])
        rec = sb("rec", [128, HALVES, C])
        drive = sb("drive", [128, KB])
        decay = sb("decay", [128, KB])
        u = sb("u", [128, KB])
        spikes = sb("spikes", [128, HALVES, STEPS, BATCH])
        out_unit = sb("out_unit", [128, HALVES * C])
        out_row = sb("out_row", [128, HALVES * C])

        ig_ps, f_ps, o_ps = bank("ig_ps"), bank("f_ps"), bank("o_ps")
        z_ps = ((ig_ps, IG), (f_ps, F), (o_ps, O))
        unit_ps, ft_bank = bank("unit_ps"), bank("ft_ps")
        igt_ps, ot_ps, c_tanh = unit_ps[:, 0:2 * HB], unit_ps[:, 2 * HB:3 * HB], unit_ps[:, 3 * HB:3 * HB + KB]
        ft_ps = ft_bank[:, 0:HB]
        scan = ft_bank[:, HB:HB + 3 * KB].rearrange("p (m s) -> p m s", s=3)
        xw_ps, wy_ps, rec_ps = bank("xw_ps"), bank("wy_ps"), bank("rec_ps")

        first_in = sem("first_in")
        weights_in = sem("weights_in")
        setup = sem("setup")
        setup_done = sem("setup_done")
        select_ready = sem("select_ready")
        x_in = sem("x_in")
        x_turned = sem("x_turned")
        x_kept = sem("x_kept")
        xw_multiplied = sem("xw_multiplied")
        xw_summed = sem("xw_summed")
        xw_split = sem("xw_split")
        xw_moved = sem("xw_moved")
        xw_free = sem("xw_free")
        xw_ready = sem("xw_ready")
        ig_summed = sem("ig_summed")
        f_summed = sem("f_summed")
        o_summed = sem("o_summed")
        igt_ready = sem("igt_ready")
        ft_ready = sem("ft_ready")
        ot_ready = sem("ot_ready")
        ig_ready = sem("ig_ready")
        scan_ready = sem("scan_ready")
        c_ready = sem("c_ready")
        tanh_ready = sem("tanh_ready")
        h_ready = sem("h_ready")
        h_halved = sem("h_halved")
        y_ready = sem("y_ready")
        y_kept = sem("y_kept")
        wy_summed = sem("wy_summed")
        wy_ready = sem("wy_ready")
        rec_summed = sem("rec_summed")
        decay_ready = sem("decay_ready")
        u_parts = sem("u_parts")
        u_ready = sem("u_ready")
        s_ready = sem("s_ready")
        out_summed = sem("out_summed")
        out_ready = sem("out_ready")
        out_stored = sem("out_stored")

        def product(ps, rows, left, w, start, lo=0, hi=HB):
            for k in range(HALVES):
                for j in range(GROUPS):
                    last = nc.tensor.matmul(ps[C * j:C * j + rows, 0:hi - lo], left(k), w[:, k, j, lo:hi],
                                            start=start and k == 0, stop=k == HALVES - 1,
                                            skip_group_check=True)
            return last

        def y_product(k):
            for j in range(GROUPS):
                last = nc.tensor.matmul(wy_ps[C * j:C * (j + 1), 0:HB], y_new[:, C * k:C * (k + 1)],
                                        wt_sb[:, k, j, :], start=k == 0, stop=k == HALVES - 1,
                                        skip_group_check=True)
            return last

        def x_product(k, lo, hi):
            for j in range(GROUPS):
                last = nc.tensor.matmul(xw_ps[C * j:C * (j + 1), lo:hi], xt_next[:, C * k:C * (k + 1)],
                                        wx_sb[:, k, j, lo:hi], start=k == 0, stop=k == HALVES - 1,
                                        skip_group_check=True)
            return last

        def pe_chunk(pe, lstm, spiking, more, t0):
            for s in range(STEPS):
                t = t0 + s
                if lstm:
                    pe.wait_ge(h_ready, t + 1)
                    h = h_first if isinstance(t, int) and t == 0 else None
                    prev = (s - 1) % STEPS
                    left = (lambda k: h_first[:, BATCH * k:BATCH * (k + 1)]) if h is not None else \
                        (lambda k: h_chunk[:, k, prev, :])
                    for (ps, gate), signal in zip(z_ps, (ig_summed, f_summed, o_summed)):
                        product(ps, BATCH, left, wh_sb, False, *gate).then_inc(signal, 1)
                if spiking:
                    vv = t - STEPS
                    pe.wait_ge(s_ready, vv + 1)
                    if isinstance(vv, int) and vv == 0:
                        left = lambda k: cond_sb[:, BATCH * k:BATCH * (k + 1)]
                    else:
                        prev_s = (s - 1) % STEPS
                        left = lambda k: spikes[:, k, prev_s, :]
                    product(rec_ps, BATCH, left, v_sb, True).then_inc(rec_summed, 1)
                if lstm and more and 0 <= s - PRODUCT_SLOT < len(PIECES):
                    if s == PRODUCT_SLOT:
                        pe.wait_ge(x_turned, t0 + 2 * STEPS)
                    k, lo, hi = PIECES[s - PRODUCT_SLOT]
                    last = x_product(k, lo, hi)
                    if s - PRODUCT_SLOT == len(PIECES) - 1:
                        last.then_inc(xw_multiplied, STEPS)
                if spiking and s == 0:
                    pe.wait_ge(y_ready, t)
                    if lstm:
                        y_product(0)
                if lstm and (more or s < STEPS - 1):
                    if s == STEPS - 1:
                        pe.wait_ge(xw_ready, t0 + 2 * STEPS)
                    last = pe_pick(pe, s + 1, t)
                    if s == STEPS - 2:
                        last.then_inc(xw_free, STEPS)
                if spiking and s == 0:
                    for k in range(1 if lstm else 0, HALVES):
                        last = y_product(k)
                    last.then_inc(wy_summed, STEPS)

        def pe_pick(pe, s, done=None):
            row = BATCH * (s % STEPS)
            for ps, (lo, hi) in z_ps:
                if done is not None:
                    pe.wait_ge(ot_ready if ps is o_ps else ft_ready, done + 1)
                for j in range(GROUPS):
                    last = nc.tensor.matmul(ps[C * j:C * j + BATCH, 0:hi - lo],
                                            select_bf[:, row:row + BATCH], xw[:, j, lo:hi],
                                            start=True, stop=False, skip_group_check=True)
            return last

        def dve_spike(dve, s, vv):
            dve.wait_ge(rec_summed, vv + 1)
            nc.vector.transpose(rec[:, :, :].rearrange("p k c -> p (k c)"),
                                rec_ps[:, 0:HALVES * C]).then_inc(u_parts, 1)
            dve.wait_ge(u_parts, 2 * (vv + 1))
            nc.vector.tensor_tensor(u[:, :].rearrange("p (k b) -> p k b", b=BATCH), rec[:, :, 0:BATCH],
                                    drive[:, :].rearrange("p (k b) -> p k b", b=BATCH),
                                    ALU.add).then_inc(u_ready, 1)
            dve.wait_ge(u_ready, vv + 2)
            nc.vector.tensor_scalar(spikes[:, :, s, :], u[:, :].rearrange("p (k b) -> p k b", b=BATCH),
                                    THRESHOLD, None, ALU.is_gt).then_inc(s_ready, 1)

        def dve_out(dve, step):
            dve.wait_ge(out_summed, step)
            nc.vector.transpose(out_row[:, :], out_unit[:, :]).then_inc(out_ready, STEPS)

        def dve_sum_xw(dve, step, n):
            dve.wait_ge(xw_multiplied, step)
            half = slice(n * (ZW // 2), (n + 1) * (ZW // 2))
            nc.vector.tensor_tensor(xw_sum[:, half], xw_ps[:, half], bias_sb[:, half],
                                    ALU.add).then_inc(xw_summed, STEPS // 2)

        def dve_turn_x(dve, step):
            dve.wait_ge(x_in, step)
            nc.vector.transpose(xt_next[:, :], x_row[:, :]).then_inc(x_turned, STEPS)

        def dve_lstm(dve, s, t):
            for (ps, (lo, hi)), unit, summed, ready in (
                    (z_ps[0], igt_ps, ig_summed, igt_ready), (z_ps[1], ft_ps, f_summed, ft_ready)):
                dve.wait_ge(summed, t + 1)
                nc.vector.transpose(unit, ps[:, 0:hi - lo]).then_inc(ready, 1)
            dve.wait_ge(ig_ready, t + 1)
            nc.vector.scalar_tensor_tensor(out=scan_add[:, :, 2], in0=gates_ig[:, 0, :], scalar=1.0,
                                           in1=gates_ig[:, 1, :], op0=ALU.add,
                                           op1=ALU.mult).then_inc(scan_ready, 1)
            dve.wait_ge(o_summed, t + 1)
            nc.vector.transpose(ot_ps, o_ps[:, 0:HB]).then_inc(ot_ready, 1)
            dve.wait_ge(scan_ready, 3 * (t + 1))
            nc.vector.tensor_tensor_scan(ft_bank[:, HB:HB + 3 * KB],
                                         scan_mul[:, :, :].rearrange("p m s -> p (m s)"),
                                         scan_add[:, :, :].rearrange("p m s -> p (m s)"),
                                         0.0, ALU.mult, ALU.add).then_inc(c_ready, 1)
            dve.wait_ge(tanh_ready, t + 1)
            nc.vector.scalar_tensor_tensor(
                out=h_chunk[:, :, s, :],
                in0=gate_o[:, :].rearrange("p (k b) -> p k b", b=BATCH), scalar=1.0,
                in1=c_tanh.rearrange("p (k b) -> p k b", b=BATCH), op0=ALU.add,
                op1=ALU.mult).then_inc(h_ready, 1)
            nc.vector.tensor_scalar(scan_add[:, :, 0:2], scan[:, :, 2:3].to_broadcast([128, KB, 2]),
                                    0.5, None, ALU.mult).then_inc(scan_ready, 1)

        def dve_chunk(dve, lstm, spiking, ending, more, t0, ready=None):
            out_due = ending
            for s in range(STEPS):
                t = t0 + s
                if spiking and s == 1:
                    dve.wait_ge(wy_summed, t0)
                    nc.vector.transpose(wy[:, :, :, :].rearrange("p k s b -> p (k s b)"),
                                        wy_ps[:, 0:HALVES * C]).then_inc(wy_ready, STEPS)
                    if ending:
                        dve.wait_ge(out_summed, t0 - STEPS)
                if (spiking and s > 0) or ending:
                    dve_spike(dve, (s - 1) % STEPS, t - STEPS - 1)
                if out_due and s == OUT_SLOT:
                    if ready is not None:
                        dve.wait_ge(out_stored, ready)
                    dve_out(dve, t0 - STEPS)
                ending = ending and s < 1
                if lstm and more and s == TURN_SLOT:
                    dve.wait_ge(x_kept, t0 + STEPS)
                    dve_turn_x(dve, t0 + 2 * STEPS)
                if lstm and more and s in (SUM_SLOT, SUM_SLOT + 1):
                    dve.wait_ge(xw_split, t0 + STEPS)
                    dve_sum_xw(dve, t0 + 2 * STEPS, s - SUM_SLOT)
                if lstm:
                    if s == 0 and spiking:
                        dve.wait_ge(h_halved, t0)
                    dve_lstm(dve, s, t)

        def act_xw(act, step):
            act.wait_ge(xw_moved, MOVES * step)
            nc.scalar.copy(xw[:, :, :], xw_next[:, :, :]).then_inc(xw_ready, STEPS)

        def act_chunk(act, more, t0):
            for s in range(STEPS):
                t = t0 + s
                if more and s == STEPS - 1:
                    act.wait_ge(xw_free, t0 + STEPS)
                    act_xw(act, t0 + 2 * STEPS)

                def batch_rows(unit):
                    return unit.rearrange("p (m r) -> p m r", r=C)[:, :, 0:BATCH]

                act.wait_ge(igt_ready, t + 1)
                nc.scalar.activation(gates_ig[:, :, :].rearrange("p g (k b) -> p (g k) b", b=BATCH),
                                     batch_rows(igt_ps), ACT.Tanh).then_inc(ig_ready, 1)
                act.wait_ge(ft_ready, t + 1)
                nc.scalar.activation(scan_mul[:, :, 1].rearrange("p (k b) -> p k b", b=BATCH),
                                     batch_rows(ft_ps), ACT.Tanh).then_inc(scan_ready, 1)
                act.wait_ge(ot_ready, t + 1)
                nc.scalar.activation(gate_o[:, :].rearrange("p (k b) -> p k b", b=BATCH),
                                     batch_rows(ot_ps), ACT.Tanh)
                act.wait_ge(c_ready, t + 1)
                nc.scalar.activation(c_tanh, scan[:, :, 2], ACT.Tanh, scale=0.5).then_inc(tanh_ready, 1)

        def pool_drive(pool, s, vv):
            pool.wait_ge(u_ready, vv + 1)
            nc.gpsimd.tensor_tensor(decay[:, :], u[:, :], a_unit[:, :], ALU.mult).then_inc(decay_ready, 1)
            if s == 0:
                pool.wait_ge(wy_ready, vv + STEPS)
            pool.wait_ge(decay_ready, vv + 1)
            nc.gpsimd.tensor_tensor(drive[:, :].rearrange("p (k b) -> p k b", b=BATCH),
                                    decay[:, :].rearrange("p (k b) -> p k b", b=BATCH),
                                    wy[:, :, s, :], ALU.add).then_inc(u_parts, 1)

        def pool_out(pool, step):
            pool.wait_ge(s_ready, step + 1)
            nc.gpsimd.tensor_tensor(out_unit[:, :], y_old[:, :],
                                    spikes[:, :, :, :].rearrange("p k s b -> p (k s b)"),
                                    ALU.add).then_inc(out_summed, STEPS)

        def pool_keep_x(pool, t0):
            pool.wait_ge(x_turned, t0 + STEPS)
            nc.gpsimd.tensor_copy(xt_now[:, :], xt_next[:, :]).then_inc(x_kept, STEPS)

        def pool_split(pool, n, step):
            part = [xw_parts[:, i, :] for i in range(PARTS)]
            if n == 0:
                pool.wait_ge(xw_summed, step)
                if not (isinstance(step, int) and step == STEPS):
                    pool.wait_ge(xw_moved, MOVES * (step - STEPS))
                now = nc.gpsimd.tensor_copy(part[0], xw_sum[:, :])
            else:
                pool.wait_ge(xw_split, step - STEPS + n * SPLIT_COUNT)
                now = (nc.gpsimd.tensor_tensor(xw_rest[:, :], xw_sum[:, :], part[0], ALU.subtract) if n == 1
                       else nc.gpsimd.tensor_copy(part[1], xw_rest[:, :]) if n == 2
                       else nc.gpsimd.tensor_tensor(part[2], xw_rest[:, :], part[1], ALU.subtract))
            now.then_inc(xw_split, SPLIT_COUNT)

        def pool_chunk(pool, lstm, ending, more, t0):
            pool.wait_ge(h_ready, t0 + 1)
            nc.gpsimd.tensor_scalar(h_half[:, :], h_chunk[:, :, :, :].rearrange("p k s b -> p (k s b)"),
                                    0.5, None, ALU.mult).then_inc(h_halved, STEPS)
            pool.wait_ge(h_halved, t0)
            nc.gpsimd.tensor_tensor(y_new[:, :], h_half[:, :], xt_now[:, :], ALU.add).then_inc(y_ready, STEPS)
            pool.wait_ge(y_ready, t0)
            if lstm:
                pool_keep_x(pool, t0)
            if ending:
                pool_out(pool, t0 - STEPS)
                pool.wait_ge(out_summed, t0 - STEPS)
            nc.gpsimd.tensor_copy(y_old[:, :], y_new[:, :]).then_inc(y_kept, STEPS)
            for s in range(STEPS):
                pool_drive(pool, s, t0 - STEPS + s)
                if more and 0 <= s - SPLIT_SLOT <= PARTS:
                    pool_split(pool, s - SPLIT_SLOT, t0 + 2 * STEPS)

        block = ctx.enter_context(nc.Block())

        @block.sync
        def _(sp):
            x_of = x.rearrange("(m p) n -> m p n", p=128)
            out_of = out.rearrange("(m p) n -> m p n", p=128)

            def load_x(m):
                sp.dma_start(x_row[:, :], x_of[m]).then_inc(x_in, 16)

            load_x(0)
            for dst, src, signal in ((wx_sb, wx, first_in), (wh_sb, wh, weights_in),
                                     (wt_sb, wt, weights_in), (v_sb, v, weights_in)):
                sp.dma_start(dst[:], src.rearrange("p (k j n) -> p k j n", k=HALVES,
                                                   j=GROUPS)).then_inc(signal, 16)
            def move_parts(m):
                for i in range(PARTS):
                    sp.wait_ge(xw_split, m * STEPS + SPLIT_DONE[i] * SPLIT_COUNT)
                    for j in range(GROUPS):
                        sp.dma_start(xw_next[C * i:C * (i + 1), j, :],
                                     xw_parts[C * j:C * (j + 1), i, :]).then_inc(xw_moved, 16)

            for m in (0, 1):
                sp.wait_ge(x_turned, (m + 1) * STEPS)
                load_x(m + 1)
                move_parts(m)
            with sp.Fori(2, CHUNKS - 1) as m:
                sp.wait_ge(x_turned, (m + 1) * STEPS)
                load_x(m + 1)
                move_parts(m)
                sp.wait_ge(out_ready, (m - 1) * STEPS)
                sp.dma_start(out_of[m - 2], out_row[:, :]).then_inc(out_stored, 16)
            move_parts(CHUNKS - 1)
            for m in range(CHUNKS - 3, CHUNKS):
                sp.wait_ge(out_ready, STEPS * (m + 1))
                sp.dma_start(out_of[m], out_row[:, :]).then_inc(out_stored, 16)
            sp.wait_ge(out_stored, 16 * CHUNKS)

        @block.gpsimd
        def _(pool):
            pool_keep_x(pool, 0)
            pool.wait_ge(x_kept, STEPS)
            for step in (STEPS, 2 * STEPS):
                for n in range(PARTS + 1):
                    pool_split(pool, n, step)
            pool_chunk(pool, True, False, True, STEPS)
            with chunk_loop(mybir.EngineType.Pool, LOOP_END) as t0:
                for first in (t0, t0 + STEPS):
                    pool_chunk(pool, True, True, True, first)
            pool_chunk(pool, True, True, True, LOOP_END)
            pool_chunk(pool, True, True, False, TIME - STEPS)
            pool_chunk(pool, False, True, False, TIME)
            pool_out(pool, TIME)

        @block.scalar
        def _(act):
            for dst, src in ((bias_sb, bias), (select_sb, select), (cond_sb, cond), (a_raw, alpha_unit),
                             (a_row, alpha_row), (eye_sb, eye), (noteye_sb, noteye)):
                if dst is bias_sb:
                    for j in range(GROUPS):
                        act.dma_start(dst[C * j:C * (j + 1), :],
                                      src[j:j + 1, :].to_broadcast([C, ZW])).then_inc(first_in, 16)
                elif dst is a_row:
                    act.dma_start(dst[:, :, :].rearrange("p j n -> p (j n)"),
                                  src.to_broadcast([128, HID])).then_inc(weights_in, 16)
                elif len(dst.shape) == 4:
                    act.dma_start(dst[:], src.rearrange("p (k j n) -> p k j n", k=HALVES,
                                                        j=GROUPS)).then_inc(weights_in, 16)
                else:
                    act.dma_start(dst[:, :], src).then_inc(weights_in, 16)
            act_xw(act, STEPS)
            act_chunk(act, True, 0)
            act_chunk(act, True, STEPS)
            with chunk_loop(mybir.EngineType.Activation, LOOP_END) as t0:
                for first in (t0, t0 + STEPS):
                    act_chunk(act, True, first)
            act_chunk(act, True, LOOP_END)
            act_chunk(act, False, TIME - STEPS)

        @block.vector
        def _(dve):
            n = 0
            for ps in (ig_ps, f_ps, o_ps, rec_ps):
                nc.vector.memset(ps[:, :], 0.0).then_inc(setup, 1)
                n += 1
            nc.vector.memset(scan_add[:, :, :], 0.0).then_inc(scan_ready, 1)
            nc.vector.memset(scan_mul[:, :, 0:2], 0.0).then_inc(setup, 1)
            nc.vector.memset(scan_mul[:, :, 2], 1.0).then_inc(setup, 1)
            n += 2
            dve_turn_x(dve, STEPS)
            dve.wait_ge(first_in, 16 * (1 + GROUPS))
            for w, f_sigmoid, f_tanh in ((bias_sb, 0.5, 1.0), (wx_sb, 0.5, 1.0), (wh_sb, 0.25, 0.5)):
                rows = w[:, :] if w is bias_sb else w[:, :, :, :].rearrange("p k j n -> p (k j) n")
                for lo, hi, f in ((0, HB, f_sigmoid), (HB, 2 * HB, f_tanh), (2 * HB, ZW, f_sigmoid)):
                    if f != 1.0:
                        part = rows[..., lo:hi]
                        nc.vector.tensor_scalar(part, part, f, None, ALU.mult).then_inc(setup, 1)
                        n += 1
                if w is wx_sb:
                    dve.wait_ge(setup, n)
                    nc.vector.sem_inc(setup_done, 1)
                    for half in range(2):
                        dve_sum_xw(dve, STEPS, half)
                    dve.wait_ge(weights_in, 16 * 9)
            nc.vector.tensor_scalar(h_first[:, :], cond_sb[:, :], 2.0, None, ALU.mult).then_inc(setup, 1)
            nc.vector.tensor_copy(u[:, :], cond_sb[:, :]).then_inc(setup, 1)
            nc.vector.tensor_copy(select_bf[:, :], select_sb[:, :]).then_inc(setup, 1)
            nc.vector.tensor_scalar(a_row[:], a_row[:], ALPHA_LO, ALPHA_HI, ALU.max,
                                    ALU.min).then_inc(setup, 1)
            nc.vector.tensor_scalar(
                a_unit[:, :].rearrange("p (k b) -> p k b", b=BATCH),
                a_raw[:, :].unsqueeze(2).to_broadcast([128, HALVES, BATCH]), ALPHA_LO, ALPHA_HI,
                ALU.max, ALU.min).then_inc(setup, 1)
            n += 5
            dve.wait_ge(setup, n)
            nc.vector.sem_inc(select_ready, 1)
            nc.vector.tensor_scalar(oma_row[:], a_row[:], -1.0, 1.0, ALU.mult, ALU.add).then_inc(setup, 1)
            nc.vector.tensor_tensor(v_sb[:], v_sb[:], noteye_sb[:], ALU.mult).then_inc(setup, 1)
            n += 2
            dve.wait_ge(setup, n)
            for k in range(HALVES):
                nc.vector.tensor_tensor(wt_sb[:, k], wt_sb[:, k], oma_row[:], ALU.mult).then_inc(setup, 1)
                nc.vector.tensor_tensor(v_sb[:, k], v_sb[:, k], oma_row[:], ALU.mult).then_inc(setup, 1)
                nc.vector.tensor_tensor(eye_sb[:, k], eye_sb[:, k], a_row[:], ALU.mult).then_inc(setup, 1)
                n += 3
            dve.wait_ge(setup, n)
            nc.vector.tensor_tensor(v_sb[:], v_sb[:], eye_sb[:], ALU.subtract).then_inc(setup, 1)
            dve.wait_ge(setup, n + 1)
            for signal in (h_ready, u_ready, s_ready):
                nc.vector.sem_inc(signal, 1)
            dve_chunk(dve, True, False, False, True, 0)
            dve_chunk(dve, True, True, False, True, STEPS)
            with chunk_loop(mybir.EngineType.DVE, LOOP_END) as t0:
                for first in (t0, t0 + STEPS):
                    dve_chunk(dve, True, True, True, True, first, first - 2 * STEPS)
            dve_chunk(dve, True, True, True, True, LOOP_END, LOOP_END - 2 * STEPS)
            dve_chunk(dve, True, True, True, False, TIME - STEPS, TIME - 3 * STEPS)
            dve_chunk(dve, False, True, True, False, TIME, TIME - 2 * STEPS)
            dve_spike(dve, STEPS - 1, TIME - 1)
            dve.wait_ge(out_stored, TIME - STEPS)
            dve_out(dve, TIME)

        @block.tensor
        def _(pe):
            pe.wait_ge(setup_done, 1)
            pe.wait_ge(x_turned, STEPS)
            for k, lo, hi in PIECES:
                last = x_product(k, lo, hi)
            last.then_inc(xw_multiplied, STEPS)
            pe.wait_ge(xw_ready, STEPS)
            pe.wait_ge(select_ready, 1)
            pe_pick(pe, 0)
            pe_chunk(pe, True, False, True, 0)
            pe_chunk(pe, True, True, True, STEPS)
            with chunk_loop(mybir.EngineType.PE, LOOP_END) as t0:
                for first in (t0, t0 + STEPS):
                    pe_chunk(pe, True, True, True, first)
            pe_chunk(pe, True, True, True, LOOP_END)
            pe_chunk(pe, True, True, False, TIME - STEPS)
            pe_chunk(pe, False, True, False, TIME)


def kernel(x, cond_1024, L0_cond_Wx, L0_cond_Wh, L0_cond_b, L1_cond_W, L1_cond_V, L1_cond_alpha):
    import concourse.bacc as bacc
    from concourse.bass_utils import run_bass_kernel_spmd

    def units(a):
        return a.reshape(GROUPS, HALVES, C, -1).transpose(0, 2, 1, 3).reshape(128, -1)

    def lstm_weights(w):
        return units(w.reshape(HID, GATES, GROUPS, HB)[:, ORDER].transpose(0, 2, 1, 3).reshape(HID, -1))

    x, cond, wx, wh, b, w, v, alpha = (np.asarray(a) for a in (
        x, cond_1024, L0_cond_Wx, L0_cond_Wh, L0_cond_b, L1_cond_W, L1_cond_V, L1_cond_alpha))
    eye = np.eye(HID, dtype=np.float32)
    arrays = {
        "x": x.reshape(BATCH, CHUNKS, STEPS, GROUPS, HB).transpose(1, 3, 2, 0, 4).reshape(CHUNKS * 128, HB),
        "cond": units(cond.T),
        "wx": lstm_weights(wx),
        "wh": lstm_weights(wh),
        "bias": b.reshape(GATES, GROUPS, HB)[ORDER].transpose(1, 0, 2).reshape(GROUPS, ZW),
        "wt": units(w.T),
        "v": units(v),
        "eye": units(eye),
        "noteye": units(1.0 - eye),
        "select": np.tile(np.eye(C, dtype=np.float32), (PARTS, 1)),
        "alpha_row": alpha.reshape(1, HID),
        "alpha_unit": units(alpha.reshape(HID, 1)),
    }
    arrays = {name: np.ascontiguousarray(a) for name, a in arrays.items()}
    nc = bacc.Bacc("TRN2", target_bir_lowering=False, num_devices=1)
    args = {name: nc.dram_tensor(name, a.shape, F32, kind="ExternalInput").ap() for name, a in arrays.items()}
    out = nc.dram_tensor("out", (CHUNKS * 128, HB), F32, kind="ExternalOutput").ap()
    build(nc, out=out, **args)
    result = run_bass_kernel_spmd(nc, [arrays], core_ids=[0]).results[0]["out"]
    return result.reshape(CHUNKS, GROUPS, STEPS, BATCH, HB).transpose(3, 0, 2, 1, 4).reshape(BATCH, TIME, HID)
```
